# Optimizing a Trainium2 kernel written in Bass

```python
import numpy as np
import jax
import jax.numpy as jnp

def _softmax(x, axis=-1):
    return jax.nn.softmax(x, axis=axis)

def _gelu(x):
    return jax.nn.gelu(x, approximate=True)

def _silu(x):
    return jax.nn.silu(x)

def _sigmoid(x):
    return jax.nn.sigmoid(x)

def _layernorm(x, axis=-1, eps=1e-05):
    m = jnp.mean(x, axis=axis, keepdims=True)
    v = jnp.var(x, axis=axis, keepdims=True)
    return (x - m) / jnp.sqrt(v + eps)

def _scatter_add(tgt, idx, src, axis=0):
    return tgt.at[idx].add(src)

def _segment_sum(src, seg, n):
    return jax.ops.segment_sum(src, seg, n)
kernel_name = 'mk_adj_preln_d1_adj_r2_b00a43'

def setup_inputs(seed: int=0):
    np.random.seed(seed)
    _w = jnp.asarray

    def _rec_inputs():
        import jax
        import jax.numpy as jnp
        _gk = jax.random.key(seed)
        x = 0.0001732 + 1 * jax.random.normal(jax.random.fold_in(_gk, 1), (5120, 64), jnp.float32)
        _a = jax.random.bernoulli(jax.random.fold_in(_gk, 2), 0.00078125, (5120, 5120))
        _af = _a.astype(jnp.float32)
        _af = _af * jax.random.uniform(jax.random.fold_in(_gk, 3), (5120, 5120), jnp.float32, 0.05, 0.02)
        adj = _af
        return (x, adj)
    x, adj = _rec_inputs()

    def _L0_gnn_setup():
        import jax, jax.numpy as jnp
        import numpy as np
        N_USERS = 2048
        N_ITEMS = 3072
        EMB = 64
        LN_EPS = 1e-05
        key = jax.random.key(seed)
        ks = jax.random.split(key, 10)
        N = N_USERS + N_ITEMS
        ego = jax.random.normal(ks[0], (N, EMB), jnp.float32)
        adj = (jax.random.uniform(ks[1], (N, N), jnp.float32) < 0.01).astype(jnp.float32) * 0.02
        xav = float(np.sqrt(6.0 / (EMB + EMB)))
        W_u = jax.random.uniform(ks[2], (EMB, EMB), jnp.float32, -xav, xav)
        W_i = jax.random.uniform(ks[3], (EMB, EMB), jnp.float32, -xav, xav)
        diag_u = jax.random.uniform(ks[4], (N_USERS,), jnp.float32, 0.99, 1.01)
        diag_i = jax.random.uniform(ks[5], (N_ITEMS,), jnp.float32, 0.99, 1.01)
        par_u = jax.random.uniform(ks[6], (2,), jnp.float32, 0.0, 0.99)
        par_i = jax.random.uniform(ks[7], (2,), jnp.float32, 0.0, 0.99)
        ln_gamma = jnp.ones((EMB,), jnp.float32)
        ln_beta = jnp.zeros((EMB,), jnp.float32)
        return {'ego_embeddings': ego, 'adj': adj, 'W_u': W_u, 'diag_u': diag_u, 'par_u': par_u, 'W_i': W_i, 'diag_i': diag_i, 'par_i': par_i, 'ln_gamma': ln_gamma, 'ln_beta': ln_beta}
    _L0_gnn_all = _L0_gnn_setup()
    _L0_gnn_in = {k: v for k, v in _L0_gnn_all.items() if k in ('W_u', 'diag_u', 'par_u', 'W_i', 'diag_i', 'par_i', 'ln_gamma', 'ln_beta')}
    del _L0_gnn_all
    return {'x': x, 'adj': adj, 'L0_gnn_W_u': _L0_gnn_in['W_u'], 'L0_gnn_diag_u': _L0_gnn_in['diag_u'], 'L0_gnn_par_u': _L0_gnn_in['par_u'], 'L0_gnn_W_i': _L0_gnn_in['W_i'], 'L0_gnn_diag_i': _L0_gnn_in['diag_i'], 'L0_gnn_par_i': _L0_gnn_in['par_i'], 'L0_gnn_ln_gamma': _L0_gnn_in['ln_gamma'], 'L0_gnn_ln_beta': _L0_gnn_in['ln_beta']}

def reference(x, adj, L0_gnn_W_u, L0_gnn_diag_u, L0_gnn_par_u, L0_gnn_W_i, L0_gnn_diag_i, L0_gnn_par_i, L0_gnn_ln_gamma, L0_gnn_ln_beta):
    import jax
    import jax.numpy as jnp

    def _L0_gnn_ref(ego_embeddings, adj, W_u, diag_u, par_u, W_i, diag_i, par_i, ln_gamma, ln_beta):
        import jax, jax.numpy as jnp
        import numpy as np
        N_USERS = 2048
        N_ITEMS = 3072
        EMB = 64
        LN_EPS = 1e-05
        nu = diag_u.shape[0]
        res = ego_embeddings
        ego_u = ego_embeddings[:nu]
        ego_i = ego_embeddings[nu:]
        u = par_u[0] * par_u[1] * (diag_u[:, None] * ego_u @ W_u) + ego_u
        i = par_i[0] * par_i[1] * (diag_i[:, None] * ego_i @ W_i) + ego_i
        e = jnp.concatenate([u, i], axis=0)
        h = adj @ (adj.T @ e)
        mu = jnp.mean(h, axis=-1, keepdims=True)
        var = jnp.var(h, axis=-1, keepdims=True)
        out = (h - mu) * jax.lax.rsqrt(var + LN_EPS) * ln_gamma + ln_beta + res
        return out
    h = jnp.maximum(_layernorm(x, axis=-1), 0.0)
    x = x + _L0_gnn_ref(h, adj, L0_gnn_W_u, L0_gnn_diag_u, L0_gnn_par_u, L0_gnn_W_i, L0_gnn_diag_i, L0_gnn_par_i, L0_gnn_ln_gamma, L0_gnn_ln_beta)
    return x

_drawn_inputs = setup_inputs


def setup_inputs(seed=0):
    import zlib

    import numpy as np

    out = dict(_drawn_inputs(seed))
    spreads = {'L0_gnn_ln_gamma': (1.0, 0.2), 'L0_gnn_ln_beta': (0.0, 0.1)}
    factors = {'L0_gnn_diag_u': 8.0, 'L0_gnn_W_i': 2.767, 'L0_gnn_diag_i': 8.0}
    for name, (base, spread) in spreads.items():
        noise = np.random.default_rng([zlib.crc32(name.encode()), seed]).standard_normal(out[name].shape)
        drawn = base * np.exp(spread * noise) if base else spread * noise
        out[name] = jnp.asarray(drawn.astype(out[name].dtype))
    for name, factor in factors.items():
        out[name] = (out[name] * factor).astype(out[name].dtype)
    return out
```

```python
import concourse.bass as bass
from concourse import mybir
from contextlib import ExitStack


def gnn_layer_kernel(nc, x, adj, W_u, diag_u, par_u, W_i, diag_i, par_i, gamma, beta, out):
    fp32 = mybir.dt.float32
    ALU = mybir.AluOpType
    ACT = mybir.ActivationFunctionType
    AX = mybir.AxisListType

    P = 128
    Q = 32
    NQ = P // Q
    N, D = x.shape
    BANK = 512
    ROWS = BANK
    GROUPS = N // ROWS
    PAIRS = GROUPS // 2
    RB = ROWS // P
    WIDTH = 2 * BANK
    PANELS = N // WIDTH
    BLOCKS = WIDTH // P
    SEG = WIDTH // NQ
    RETAINED = 4
    RPAIRS = RETAINED // 2
    SPAIRS = PAIRS - RPAIRS
    RING = 6
    USER_GROUPS = diag_u.shape[0] // ROWS
    USER_PAIRS = USER_GROUPS // 2
    USER_BLOCKS = USER_GROUPS * RB
    ALL_BLOCKS = GROUPS * RB
    UB = 2 * RB
    EPS = 1e-5

    ctx = ExitStack()
    with ctx:
        def sb(name, shape, dt=fp32):
            return ctx.enter_context(nc.sbuf_tensor(name, shape, dt))

        def pb(name, shape, dt=fp32):
            return ctx.enter_context(nc.psum_tensor(name, shape, dt))

        def sem(name):
            return ctx.enter_context(nc.semaphore(name))

        panel = sb("panel", [P, GROUPS, RB * WIDTH])
        x_sb = sb("x_sb", [P, ALL_BLOCKS, D])
        e_sb = sb("e_sb", [P, ALL_BLOCKS, D])
        at_ring = sb("at_ring", [P, RING, ROWS])
        tT_sb = sb("tT_sb", [D, WIDTH])
        t_blocks = sb("t_blocks", [P, BLOCKS, D])
        t_strided = sb("t_strided", [P, BLOCKS, D])
        ident = sb("ident", [P, P])
        w_blk = sb("w_blk", [P, 2, P])
        diag_rows = sb("diag_rows", [ALL_BLOCKS, P])
        par_rows = sb("par_rows", [ALL_BLOCKS, 2])
        scale_rows = sb("scale_rows", [ALL_BLOCKS, 1])
        diag_sb = sb("diag_sb", [P, ALL_BLOCKS])
        gamma_sb = sb("gamma_sb", [P, D])
        beta_sb = sb("beta_sb", [P, D])
        eps_sb = sb("eps_sb", [P, 1])
        stats = sb("stats", [P, 2 * PAIRS, 5, UB])

        h_ps = [pb(f"h_ps{k}", [P, BANK]) for k in range(PAIRS)]
        tT_ps = pb("tT_ps", [P, BANK])
        tr_ps = [pb(f"tr_ps{k}", [P, BANK]) for k in range(2)]

        x_in = [sem(f"x_in{u}") for u in range(PAIRS)]
        small_in = sem("small_in")
        w_in = sem("w_in")
        w_zeroed = sem("w_zeroed")
        eps_ready = sem("eps_ready")
        ident_ready = sem("ident_ready")
        scale_ready = sem("scale_ready")
        diag_turned = sem("diag_turned")
        diag_ready = sem("diag_ready")
        centred = sem("centred")
        squared = sem("squared")
        summed = sem("summed")
        rooted = sem("rooted")
        normed = sem("normed")
        ego_ready = sem("ego_ready")
        ego_turned = sem("ego_turned")
        egoT_ready = sem("egoT_ready")
        y_ready = sem("y_ready")
        res_summed = sem("res_summed")
        res_ready = sem("res_ready")
        e_ready = sem("e_ready")
        h_zeroed = sem("h_zeroed")
        natural_in = [sem(f"natural_in{g}") for g in range(GROUPS)]
        second_in = [sem(f"second_in{g}") for g in range(GROUPS)]
        t_summed = sem("t_summed")
        tr_filled = sem("tr_filled")
        tr_emptied = sem("tr_emptied")
        tT_ready = sem("tT_ready")
        t_turned = sem("t_turned")
        t_ready = sem("t_ready")
        at_filled = sem("at_filled")
        at_used = sem("at_used")
        h_summed = sem("h_summed")
        hT_ready = sem("hT_ready")
        h_turned = sem("h_turned")
        out_ready = sem("out_ready")
        stored = sem("stored")
        vstep = sem("vstep")
        pstep = sem("pstep")

        def slot_natural(g):
            return panel[:, g, :].rearrange("p (r c) -> p r c", r=RB)

        def slot_columns(g, b):
            return slot_natural(g)[:, :, b * P:(b + 1) * P]

        def slot_second(g, b):
            return panel[:, g, :].rearrange("p (m c b) -> p m c b", c=Q, b=BLOCKS)[:, :, :, b]

        def work(g, k):
            return panel[:, g, k * BANK:(k + 1) * BANK]

        def rows64(ap):
            return ap.rearrange("p (n d) -> p n d", d=D)

        def per_row(ap):
            return ap.rearrange("p (n o) -> p n o", o=1).to_broadcast([P, UB, D])

        def per_column(ap):
            return ap.rearrange("p (o d) -> p o d", o=1).to_broadcast([P, UB, D])

        def unit(t, u):
            return t[:, u * UB:(u + 1) * UB, :]

        def load_natural(eng, g, p):
            src = adj[g * ROWS:(g + 1) * ROWS, bass.ds(p * WIDTH, WIDTH)]
            eng.dma_start(slot_natural(g), src.rearrange("(r p) c -> p r c", p=P)).then_inc(natural_in[g], 16)

        def load_second(eng, g, p, quadrants):
            for q in quadrants:
                src = adj[g * ROWS:(g + 1) * ROWS, bass.ds(p * WIDTH + q * SEG, SEG)]
                dst = panel[q * Q:(q + 1) * Q, g, :].rearrange("p (m c) -> p m c", c=SEG)
                eng.dma_start(dst, src.rearrange("(m p) c -> p m c", p=Q)).then_inc(second_in[g], 16)

        EGO_SLOT = GROUPS - 1
        OUT_SLOT = 0

        block = ctx.enter_context(nc.Block())

        @block.sync
        def _(sp):
            def load_x(u):
                src = x[u * 2 * ROWS:(u + 1) * 2 * ROWS, :].rearrange("(n p) d -> p n d", p=P)
                sp.dma_start(unit(x_sb, u), src).then_inc(x_in[u], 16)

            load_x(0)
            load_natural(sp, 0, 0)
            for u in range(1, PAIRS):
                load_x(u)
            for g in range(1, GROUPS):
                if g == EGO_SLOT:
                    sp.wait_ge(e_ready, PAIRS)
                load_natural(sp, g, 0)

            def second_half_of_queue(p):
                for g in range(RETAINED, GROUPS):
                    sp.wait_ge(t_summed, p * GROUPS + (g + 1))
                    load_second(sp, g, p, range(0, NQ // 2))

            with sp.Fori(0, PANELS - 1) as p:
                second_half_of_queue(p)
                for g in range(GROUPS):
                    if g < RETAINED:
                        sp.wait_ge(h_summed, p * RPAIRS + (g // 2 + 1))
                    else:
                        sp.wait_ge(at_filled, p * (SPAIRS * BLOCKS) + (g // 2 - RPAIRS + 1) * BLOCKS)
                    load_natural(sp, g, p + 1)
            second_half_of_queue(PANELS - 1)
            for k in range(PAIRS):
                sp.wait_ge(out_ready, k + 1)
                for half in range(2):
                    g = 2 * k + half
                    dst = out[g * ROWS:(g + 1) * ROWS, :].rearrange("(r p) d -> p r d", p=P)
                    sp.dma_start(dst, x_sb[:, g * RB:(g + 1) * RB, :]).then_inc(stored, 16)
            sp.wait_ge(stored, 16 * 2 * PAIRS)

        @block.gpsimd
        def _(pool):
            pool.memset(w_blk[:, :, :], 0.0).then_inc(w_zeroed, 1)
            pool.memset(ident[:, :], 0.0).then_inc(pstep, 1)
            pool.wait_ge(pstep, 1)
            pool.affine_select(out=ident[:, :], in_=ident[:, :], compare_op=ALU.not_equal, fill=1.0,
                               base=0, pattern=[[-1, P]], channel_multiplier=1).then_inc(ident_ready, 1)
            pool.wait_ge(small_in, 16 * 6)
            for u in range(PAIRS):
                pool.wait_ge(ego_ready, u + 1)
                pool.tensor_tensor(unit(x_sb, u), unit(x_sb, u), unit(e_sb, u), ALU.add).then_inc(res_summed, 1)
                pool.wait_ge(res_summed, u + 1)
                pool.tensor_tensor(unit(x_sb, u), unit(x_sb, u), per_column(beta_sb[:, :]),
                                   ALU.add).then_inc(res_ready, 1)

        @block.scalar
        def _(act):
            act.dma_start(diag_rows[0:USER_BLOCKS, :], diag_u.rearrange("(n p) -> n p", p=P)).then_inc(small_in, 16)
            act.dma_start(diag_rows[USER_BLOCKS:ALL_BLOCKS, :],
                          diag_i.rearrange("(n p) -> n p", p=P)).then_inc(small_in, 16)
            act.dma_start(par_rows[0:USER_BLOCKS, :],
                          par_u.rearrange("(o n) -> o n", o=1).to_broadcast([USER_BLOCKS, 2])).then_inc(small_in, 16)
            act.dma_start(par_rows[USER_BLOCKS:ALL_BLOCKS, :],
                          par_i.rearrange("(o n) -> o n", o=1).to_broadcast([ALL_BLOCKS - USER_BLOCKS, 2])
                          ).then_inc(small_in, 16)
            act.dma_start(gamma_sb[:, :], gamma.rearrange("(o n) -> o n", o=1).to_broadcast([P, D])).then_inc(small_in, 16)
            act.dma_start(beta_sb[:, :], beta.rearrange("(o n) -> o n", o=1).to_broadcast([P, D])).then_inc(small_in, 16)
            act.wait_ge(w_zeroed, 1)
            for s, W in enumerate((W_u, W_i)):
                for half in range(2):
                    act.dma_start(w_blk[half * D:(half + 1) * D, s, half * D:(half + 1) * D], W[:, :]).then_inc(w_in, 16)

            def squares(n):
                act.wait_ge(centred, n + 1)
                slot = EGO_SLOT if n < PAIRS else OUT_SLOT
                nc.scalar.activation(work(slot, 2 + n % 2), work(slot, n % 2), ACT.Square).then_inc(squared, 1)

            def root(n):
                act.wait_ge(summed, n + 1)
                nc.scalar.activation(stats[:, n, 3, :], stats[:, n, 2, :], ACT.Sqrt,
                                     bias=eps_sb[:, 0:1], scale=1.0 / D).then_inc(rooted, 1)

            for s in range(PAIRS + 1):
                if s < PAIRS:
                    squares(s)
                    if s == 0:
                        act.wait_ge(eps_ready, 1)
                    root(s)
                    act.wait_ge(normed, s + 1)
                    nc.scalar.activation(unit(e_sb, s), rows64(work(EGO_SLOT, s % 2)), ACT.Relu).then_inc(ego_ready, 1)
                if s >= 1:
                    act.wait_ge(ego_turned, s)
                    if s >= 3:
                        act.wait_ge(y_ready, s - 2)
                    nc.scalar.activation(work(EGO_SLOT, 4 + (s - 1) % 2), tr_ps[(s - 1) % 2][:, :],
                                         ACT.Copy).then_inc(egoT_ready, 1)

            def slot_back(p, g):
                for b in range(BLOCKS):
                    n = g * BLOCKS + b
                    act.wait_ge(tr_filled, p * (RETAINED * BLOCKS) + (n + 1))
                    src = tr_ps[n % 2][:, :].rearrange("p (r c) -> p r c", r=RB)
                    nc.scalar.activation(slot_columns(g, b), src, ACT.Copy).then_inc(tr_emptied, 1)

            with act.Fori(0, PANELS) as p:
                for g in range(RETAINED - 1):
                    slot_back(p, g)
                for g in range(RETAINED, GROUPS):
                    act.wait_ge(t_summed, p * GROUPS + (g + 1))
                    load_second(act, g, p, range(NQ // 2, NQ))
                nc.scalar.activation(tT_sb[:, BANK:WIDTH], tT_ps[D:P, :], ACT.Copy).then_inc(tT_ready, 1)
                slot_back(p, RETAINED - 1)

            def hT_copy(k):
                if k < RPAIRS:
                    act.wait_ge(h_summed, (PANELS - 1) * RPAIRS + k + 1)
                else:
                    act.wait_ge(at_used, (PANELS - 1) * (SPAIRS * BLOCKS) + (k - RPAIRS + 1) * BLOCKS)
                if k >= 2:
                    act.wait_ge(h_turned, k - 1)
                nc.scalar.activation(work(OUT_SLOT, 4 + k % 2), h_ps[k][:, :], ACT.Copy).then_inc(hT_ready, 1)

            hT_copy(0)
            for k in range(PAIRS):
                if k + 1 < PAIRS:
                    hT_copy(k + 1)
                squares(PAIRS + k)
                root(PAIRS + k)

        @block.vector
        def _(dve):
            chain = [0]

            def link(ins):
                chain[0] += 1
                ins.then_inc(vstep, 1)
                dve.wait_ge(vstep, chain[0])

            nc.vector.memset(eps_sb[:, :], EPS).then_inc(eps_ready, 1)

            def centre(n, src, dst):
                link(nc.vector.reduce_sum(stats[:, n, 0, :], src, axis=AX.X))
                link(nc.vector.tensor_scalar(stats[:, n, 1, :], stats[:, n, 0, :], -1.0 / D, None, ALU.mult))
                nc.vector.tensor_tensor(dst, src, per_row(stats[:, n, 1, :]), ALU.add).then_inc(centred, 1)

            def square_sum(n, slot):
                dve.wait_ge(squared, n + 1)
                nc.vector.reduce_sum(stats[:, n, 2, :], rows64(work(slot, 2 + n % 2)), axis=AX.X).then_inc(summed, 1)

            def norm(n, slot):
                dve.wait_ge(rooted, n + 1)
                link(nc.vector.reciprocal(stats[:, n, 4, :], stats[:, n, 3, :]))
                c = rows64(work(slot, n % 2))
                return nc.vector.tensor_tensor(c, c, per_row(stats[:, n, 4, :]), ALU.mult)

            def e_rows(u):
                dve.wait_ge(y_ready, u + 1)
                y = rows64(h_ps[u][:, :])
                scaled = rows64(work(EGO_SLOT, 6))
                if u:
                    dve.wait_ge(e_ready, u)
                link(nc.vector.tensor_tensor(scaled, y, per_row(diag_sb[:, u * UB:(u + 1) * UB]), ALU.mult))
                dve.wait_ge(res_summed, u + 1)
                nc.vector.tensor_tensor(unit(e_sb, u), unit(e_sb, u), scaled, ALU.add).then_inc(e_ready, 1)
                nc.vector.memset(h_ps[u][:, :], 0.0).then_inc(h_zeroed, 1)

            for u in range(PAIRS + 2):
                if u < PAIRS:
                    dve.wait_ge(x_in[u], 16)
                    if u >= 2:
                        dve.wait_ge(ego_ready, u - 1)
                    centre(u, unit(x_sb, u), rows64(work(EGO_SLOT, u % 2)))
                if u == 0:
                    dve.wait_ge(small_in, 16 * 6)
                    link(nc.vector.tensor_tensor(scale_rows[:, :], par_rows[:, 0:1], par_rows[:, 1:2], ALU.mult))
                    nc.vector.tensor_scalar(diag_rows[:, :], diag_rows[:, :], scale_rows[:, 0:1], None,
                                            ALU.mult).then_inc(scale_ready, 1)
                if u < PAIRS:
                    square_sum(u, EGO_SLOT)
                    norm(u, EGO_SLOT).then_inc(normed, 1)
                if u == 0:
                    dve.wait_ge(diag_turned, 1)
                    link(nc.vector.tensor_copy(diag_sb[:, :], tT_ps[:, 0:ALL_BLOCKS]))
                if u >= 2:
                    e_rows(u - 2)

            with dve.Fori(0, PANELS) as p:
                dve.wait_ge(t_summed, p * GROUPS + GROUPS)
                nc.vector.tensor_copy(tT_sb[:, 0:BANK], tT_ps[0:D, :]).then_inc(tT_ready, 1)
                for n, t in enumerate((t_blocks, t_strided)):
                    dve.wait_ge(t_turned, 2 * p + (n + 1))
                    nc.vector.tensor_copy(t[:, :, :], rows64(tT_ps[:, :])).then_inc(t_ready, 1)
                for k in range(SPAIRS):
                    for g in (2 * (RPAIRS + k), 2 * (RPAIRS + k) + 1):
                        dve.wait_ge(second_in[g], p * (16 * NQ) + 16 * NQ)
                    for b in range(BLOCKS):
                        n = k * BLOCKS + b
                        if n >= RING // 2:
                            dve.wait_ge(at_used, p * (SPAIRS * BLOCKS) + (n + 1 - RING // 2))
                        for half in range(2):
                            g = 2 * (RPAIRS + k) + half
                            last = nc.vector.transpose(at_ring[:, (2 * n + half) % RING, :].rearrange("p (m c) -> p m c", c=Q),
                                                       slot_second(g, b))
                        last.then_inc(at_filled, 1)

            for k in range(PAIRS):
                n = PAIRS + k
                dve.wait_ge(h_turned, k + 1)
                if k == 0:
                    dve.wait_ge(res_ready, PAIRS)
                h = tr_ps[k % 2][:, :].rearrange("p (r h d) -> p h r d", h=2, d=D)
                stat = lambda j: stats[:, n, j, :].rearrange("p (h r) -> p h r", h=2)
                link(nc.vector.reduce_sum(stat(0), h, axis=AX.X))
                link(nc.vector.tensor_scalar(stats[:, n, 1, :], stats[:, n, 0, :], -1.0 / D, None, ALU.mult))
                nc.vector.tensor_tensor(
                    work(OUT_SLOT, n % 2).rearrange("p (h r d) -> p h r d", h=2, d=D), h,
                    stats[:, n, 1, :].rearrange("p (h r o) -> p h r o", h=2, o=1).to_broadcast([P, 2, RB, D]),
                    ALU.add).then_inc(centred, 1)
                square_sum(n, OUT_SLOT)
                link(norm(n, OUT_SLOT))
                c = rows64(work(OUT_SLOT, n % 2))
                link(nc.vector.tensor_tensor(c, c, per_column(gamma_sb[:, :]), ALU.mult))
                nc.vector.tensor_tensor(unit(x_sb, k), unit(x_sb, k), c, ALU.add).then_inc(out_ready, 1)

        @block.tensor
        def _(pe):
            pe.wait_ge(ident_ready, 1)
            pe.wait_ge(scale_ready, 1)
            nc.tensor.transpose(tT_ps[:, 0:ALL_BLOCKS], diag_rows[:, :],
                                ident[0:ALL_BLOCKS, 0:ALL_BLOCKS]).then_inc(diag_turned, 1)
            for u in range(PAIRS + 1):
                if u < PAIRS:
                    pe.wait_ge(ego_ready, u + 1)
                    if u >= 2:
                        pe.wait_ge(egoT_ready, u - 1)
                    for j in range(RB):
                        last = nc.tensor.transpose(tr_ps[u % 2][:, j * P:(j + 1) * P],
                                                   e_sb[:, u * UB + 2 * j:u * UB + 2 * j + 2, :], ident[:, :])
                    last.then_inc(ego_turned, 1)
                if u >= 1:
                    v = u - 1
                    pe.wait_ge(egoT_ready, v + 1)
                    if v == 0:
                        pe.wait_ge(w_in, 16 * 4)
                    for j in range(RB):
                        last = nc.tensor.matmul(h_ps[v][:, j * P:(j + 1) * P],
                                                work(EGO_SLOT, 4 + v % 2)[:, j * P:(j + 1) * P],
                                                w_blk[:, 0 if v < USER_PAIRS else 1, :], start=True, stop=True)
                    last.then_inc(y_ready, 1)
            def sum_t(p, g):
                pe.wait_ge(natural_in[g], p * 16 + 16)
                for rb in range(RB):
                    for half in range(2):
                        last = nc.tensor.matmul(tT_ps[half * D:(half + 1) * D, :], e_sb[:, g * RB + rb, :],
                                                slot_natural(g)[:, rb, half * BANK:(half + 1) * BANK], start=(g == 0 and rb == 0),
                                                stop=(g == GROUPS - 1 and rb == RB - 1))
                last.then_inc(t_summed, 1)

            def turn_slot(p, g, blocks):
                for b in blocks:
                    n = g * BLOCKS + b
                    if n >= 2:
                        pe.wait_ge(tr_emptied, p * (RETAINED * BLOCKS) + (n - 1))
                    for rb in range(RB):
                        last = nc.tensor.transpose(tr_ps[n % 2][:, rb * P:(rb + 1) * P],
                                                   slot_columns(g, b)[:, rb, :], ident[:, :])
                    last.then_inc(tr_filled, 1)

            def turn_t(columns):
                for b in range(BLOCKS):
                    last = nc.tensor.transpose(tT_ps[:, b * D:(b + 1) * D], columns(b), ident[0:D, 0:D])
                last.then_inc(t_turned, 1)

            def sum_h(k, b, t_sb, tiles):
                for half in range(2):
                    last = nc.tensor.matmul(h_ps[k][half * D:(half + 1) * D, :], t_sb[:, b, :], tiles[half],
                                            start=False, stop=True, skip_group_check=True)
                return last

            with pe.Fori(0, PANELS) as p:
                for g in range(GROUPS):
                    if g % 2 == 0:
                        pe.wait_ge(e_ready, g // 2 + 1)
                    sum_t(p, g)
                    if g < RETAINED - 1:
                        turn_slot(p, g, range(BLOCKS))
                turn_slot(p, RETAINED - 1, range(0, BLOCKS // 2 - 1))
                pe.wait_ge(tT_ready, 2 * p + 2)
                turn_slot(p, RETAINED - 1, range(BLOCKS // 2 - 1, BLOCKS // 2))
                turn_t(lambda b: tT_sb[:, b * P:(b + 1) * P])
                turn_slot(p, RETAINED - 1, range(BLOCKS // 2, BLOCKS))
                pe.wait_ge(t_ready, 2 * p + 1)
                pe.wait_ge(h_zeroed, PAIRS)
                for k in range(RPAIRS):
                    pe.wait_ge(tr_emptied, p * (RETAINED * BLOCKS) + (2 * k + 2) * BLOCKS)
                    for b in range(BLOCKS):
                        last = sum_h(k, b, t_blocks, [slot_columns(2 * k + half, b) for half in range(2)])
                    last.then_inc(h_summed, 1)
                    if k == 0:
                        turn_t(lambda b: tT_sb[:, :].rearrange("d (c b) -> d c b", b=BLOCKS)[:, :, b])
                pe.wait_ge(t_ready, 2 * p + 2)
                for k in range(SPAIRS):
                    for b in range(BLOCKS):
                        n = k * BLOCKS + b
                        pe.wait_ge(at_filled, p * (SPAIRS * BLOCKS) + (n + 1))
                        last = sum_h(RPAIRS + k, b, t_strided, [at_ring[:, (2 * n + half) % RING, :] for half in range(2)])
                        last.then_inc(at_used, 1)

            for k in range(PAIRS):
                pe.wait_ge(hT_ready, k + 1)
                if k >= 2:
                    pe.wait_ge(out_ready, k - 1)
                for rb in range(RB):
                    last = nc.tensor.transpose(tr_ps[k % 2][:, rb * P:(rb + 1) * P],
                                               work(OUT_SLOT, 4 + k % 2)[:, rb * P:(rb + 1) * P], ident[:, :])
                last.then_inc(h_turned, 1)


_INS = ['x', 'adj', 'L0_gnn_W_u', 'L0_gnn_diag_u', 'L0_gnn_par_u', 'L0_gnn_W_i', 'L0_gnn_diag_i',
        'L0_gnn_par_i', 'L0_gnn_ln_gamma', 'L0_gnn_ln_beta']
_OUTS = [((5120, 64), 'float32')]


def kernel(**inputs):
    import numpy as _np
    import concourse.bacc as _bacc
    from concourse import mybir as _mybir
    from concourse.bass_utils import run_bass_kernel_spmd as _run

    nc = _bacc.Bacc("TRN2", target_bir_lowering=False, num_devices=1)
    arrays, args = {}, []
    for name in _INS:
        a = _np.ascontiguousarray(inputs[name])
        arrays[f"in_{name}_dram"] = a
        args.append(nc.dram_tensor(f"in_{name}_dram", a.shape, _mybir.dt.from_np(a.dtype), kind="ExternalInput").ap())
    for i, (shape, dtype) in enumerate(_OUTS):
        dt = _mybir.dt.from_np(_np.dtype(dtype))
        args.append(nc.dram_tensor(f"out_{i}_dram", shape, dt, kind="ExternalOutput").ap())
    gnn_layer_kernel(nc, *args)
    r = _run(nc, [arrays], core_ids=[0])
    return r.results[0]["out_0_dram"]
```

```python
import concourse.bass as bass
from concourse import mybir
from contextlib import ExitStack


def gnn_layer_kernel(nc, x, adj, W_u, diag_u, par_u, W_i, diag_i, par_i, gamma, beta, out):
    fp32 = mybir.dt.float32
    ALU = mybir.AluOpType
    ACT = mybir.ActivationFunctionType
    AX = mybir.AxisListType

    P = 128
    Q = 32
    NQ = P // Q
    N, D = x.shape
    BANK = 512
    ROWS = BANK
    GROUPS = N // ROWS
    PAIRS = GROUPS // 2
    RB = ROWS // P
    WIDTH = 2 * BANK
    PANELS = N // WIDTH
    BLOCKS = WIDTH // P
    SEG = WIDTH // NQ
    RETAINED = 4
    RPAIRS = RETAINED // 2
    SPAIRS = PAIRS - RPAIRS
    RING = 6
    HELD_BACK = RETAINED - 1
    USER_GROUPS = diag_u.shape[0] // ROWS
    USER_PAIRS = USER_GROUPS // 2
    USER_BLOCKS = USER_GROUPS * RB
    ALL_BLOCKS = GROUPS * RB
    UB = 2 * RB
    EPS = 1e-5

    ctx = ExitStack()
    with ctx:
        def sb(name, shape, dt=fp32):
            return ctx.enter_context(nc.sbuf_tensor(name, shape, dt))

        def pb(name, shape, dt=fp32):
            return ctx.enter_context(nc.psum_tensor(name, shape, dt))

        def sem(name):
            return ctx.enter_context(nc.semaphore(name))

        panel = sb("panel", [P, GROUPS, RB * WIDTH])
        x_sb = sb("x_sb", [P, ALL_BLOCKS, D])
        e_sb = sb("e_sb", [P, ALL_BLOCKS, D])
        at_ring = sb("at_ring", [P, RING, 2, ROWS])
        tT_sb = sb("tT_sb", [D, WIDTH])
        t_blocks = sb("t_blocks", [P, BLOCKS, D])
        t_strided = sb("t_strided", [P, BLOCKS, D])
        ident = sb("ident", [P, P])
        w_blk = sb("w_blk", [P, 2, P])
        diag_rows = sb("diag_rows", [ALL_BLOCKS, P])
        par_rows = sb("par_rows", [ALL_BLOCKS, 2])
        scale_rows = sb("scale_rows", [ALL_BLOCKS, 1])
        diag_sb = sb("diag_sb", [P, ALL_BLOCKS])
        gamma_sb = sb("gamma_sb", [P, D])
        beta_sb = sb("beta_sb", [P, D])
        eps_sb = sb("eps_sb", [P, 1])
        root_warm = sb("root_warm", [P, 1])
        stats = sb("stats", [P, 2 * PAIRS, 5, UB])

        h_ps = [pb(f"h_ps{k}", [P, BANK]) for k in range(PAIRS)]
        tT_ps = pb("tT_ps", [P, BANK])
        tr_ps = [pb(f"tr_ps{k}", [P, BANK]) for k in range(2)]

        x_in = [sem(f"x_in{u}") for u in range(PAIRS)]
        small_in = sem("small_in")
        w_in = sem("w_in")
        w_zeroed = sem("w_zeroed")
        eps_ready = sem("eps_ready")
        ident_ready = sem("ident_ready")
        scale_ready = sem("scale_ready")
        diag_turned = sem("diag_turned")
        diag_ready = sem("diag_ready")
        centred = sem("centred")
        squared = sem("squared")
        summed = sem("summed")
        rooted = sem("rooted")
        normed = sem("normed")
        root_warmed = sem("root_warmed")
        ego_ready = sem("ego_ready")
        ego_turned = sem("ego_turned")
        egoT_ready = sem("egoT_ready")
        y_ready = sem("y_ready")
        res_summed = sem("res_summed")
        res_ready = sem("res_ready")
        e_ready = sem("e_ready")
        h_zeroed = sem("h_zeroed")
        natural_in = [sem(f"natural_in{g}") for g in range(GROUPS)]
        second_in = [sem(f"second_in{g}") for g in range(GROUPS)]
        t_summed = sem("t_summed")
        tr_filled = sem("tr_filled")
        tr_emptied = sem("tr_emptied")
        tT_ready = sem("tT_ready")
        t_turned = sem("t_turned")
        t_ready = sem("t_ready")
        at_filled = sem("at_filled")
        at_used = sem("at_used")
        h_summed = sem("h_summed")
        hT_ready = sem("hT_ready")
        h_turned = sem("h_turned")
        out_ready = sem("out_ready")
        last_out_ready = sem("last_out_ready")
        out_normed = sem("out_normed")
        out_scaled = sem("out_scaled")
        stored = sem("stored")
        vstep = sem("vstep")
        pstep = sem("pstep")

        def slot_natural(g):
            return panel[:, g, :].rearrange("p (r c) -> p r c", r=RB)

        def slot_columns(g, b):
            return slot_natural(g)[:, :, b * P:(b + 1) * P]

        def slots_second(k, b):
            pair = panel[:, 2 * k:2 * k + 2, :].rearrange("p g (m c b) -> p (g m) c b", c=Q, b=BLOCKS)
            return pair[:, :, :, b]

        def work(g, k):
            return panel[:, g, k * BANK:(k + 1) * BANK]

        def rows64(ap):
            return ap.rearrange("p (n d) -> p n d", d=D)

        def per_row(ap):
            return ap.rearrange("p (n o) -> p n o", o=1).to_broadcast([P, UB, D])

        def per_column(ap):
            return ap.rearrange("p (o d) -> p o d", o=1).to_broadcast([P, UB, D])

        def unit(t, u):
            return t[:, u * UB:(u + 1) * UB, :]

        def load_natural(eng, g, p):
            src = adj[g * ROWS:(g + 1) * ROWS, bass.ds(p * WIDTH, WIDTH)]
            eng.dma_start(slot_natural(g), src.rearrange("(r p) c -> p r c", p=P)).then_inc(natural_in[g], 16)

        def load_second(eng, g, p, quadrants):
            for q in quadrants:
                src = adj[g * ROWS:(g + 1) * ROWS, bass.ds(p * WIDTH + q * SEG, SEG)]
                dst = panel[q * Q:(q + 1) * Q, g, :].rearrange("p (m c) -> p m c", c=SEG)
                eng.dma_start(dst, src.rearrange("(m p) c -> p m c", p=Q)).then_inc(second_in[g], 16)

        EGO_SLOT = GROUPS - 1
        OUT_SLOT = 0

        block = ctx.enter_context(nc.Block())

        @block.sync
        def _(sp):
            def load_x(u):
                src = x[u * 2 * ROWS:(u + 1) * 2 * ROWS, :].rearrange("(n p) d -> p n d", p=P)
                sp.dma_start(unit(x_sb, u), src).then_inc(x_in[u], 16)

            for u in range(PAIRS):
                load_x(u)
            for g in range(GROUPS):
                if g == EGO_SLOT:
                    sp.wait_ge(e_ready, PAIRS)
                load_natural(sp, g, 0)

            def second_half_of_queue(p):
                for g in range(RETAINED, GROUPS):
                    sp.wait_ge(t_summed, p * GROUPS + (g + 1))
                    load_second(sp, g, p, range(0, NQ // 2))

            with sp.Fori(0, PANELS - 1) as p:
                second_half_of_queue(p)
                for g in range(GROUPS):
                    if g < RETAINED:
                        sp.wait_ge(h_summed, p * RPAIRS + (g // 2 + 1))
                    else:
                        sp.wait_ge(at_filled, p * (SPAIRS * BLOCKS) + (g // 2 - RPAIRS + 1) * BLOCKS)
                    load_natural(sp, g, p + 1)
            second_half_of_queue(PANELS - 1)
            for k in range(PAIRS):
                if k < PAIRS - 1:
                    sp.wait_ge(out_ready, k + 1)
                else:
                    sp.wait_ge(last_out_ready, 1)
                for half in range(2):
                    g = 2 * k + half
                    dst = out[g * ROWS:(g + 1) * ROWS, :].rearrange("(r p) d -> p r d", p=P)
                    sp.dma_start(dst, x_sb[:, g * RB:(g + 1) * RB, :]).then_inc(stored, 16)
            sp.wait_ge(stored, 16 * 2 * PAIRS)

        @block.gpsimd
        def _(pool):
            pool.memset(w_blk[:, :, :], 0.0).then_inc(w_zeroed, 1)
            pool.memset(ident[:, :], 0.0).then_inc(pstep, 1)
            pool.wait_ge(pstep, 1)
            pool.affine_select(out=ident[:, :], in_=ident[:, :], compare_op=ALU.not_equal, fill=1.0,
                               base=0, pattern=[[-1, P]], channel_multiplier=1).then_inc(ident_ready, 1)
            pool.wait_ge(small_in, 16 * 6)
            for u in range(PAIRS):
                pool.wait_ge(ego_ready, u + 1)
                pool.tensor_tensor(unit(x_sb, u), unit(x_sb, u), unit(e_sb, u), ALU.add).then_inc(res_summed, 1)
                pool.wait_ge(res_summed, u + 1)
                pool.tensor_tensor(unit(x_sb, u), unit(x_sb, u), per_column(beta_sb[:, :]),
                                   ALU.add).then_inc(res_ready, 1)
            for k in range(PAIRS - 1):
                c = rows64(work(OUT_SLOT, (PAIRS + k) % 2))
                pool.wait_ge(out_normed, k + 1)
                pool.tensor_tensor(c, c, per_column(gamma_sb[:, :]), ALU.mult).then_inc(out_scaled, 1)
                pool.wait_ge(out_scaled, k + 1)
                pool.tensor_tensor(unit(x_sb, k), unit(x_sb, k), c, ALU.add).then_inc(out_ready, 1)

        @block.scalar
        def _(act):
            act.dma_start(diag_rows[0:USER_BLOCKS, :], diag_u.rearrange("(n p) -> n p", p=P)).then_inc(small_in, 16)
            act.dma_start(diag_rows[USER_BLOCKS:ALL_BLOCKS, :],
                          diag_i.rearrange("(n p) -> n p", p=P)).then_inc(small_in, 16)
            act.dma_start(par_rows[0:USER_BLOCKS, :],
                          par_u.rearrange("(o n) -> o n", o=1).to_broadcast([USER_BLOCKS, 2])).then_inc(small_in, 16)
            act.dma_start(par_rows[USER_BLOCKS:ALL_BLOCKS, :],
                          par_i.rearrange("(o n) -> o n", o=1).to_broadcast([ALL_BLOCKS - USER_BLOCKS, 2])
                          ).then_inc(small_in, 16)
            act.dma_start(gamma_sb[:, :], gamma.rearrange("(o n) -> o n", o=1).to_broadcast([P, D])).then_inc(small_in, 16)
            act.dma_start(beta_sb[:, :], beta.rearrange("(o n) -> o n", o=1).to_broadcast([P, D])).then_inc(small_in, 16)
            act.wait_ge(w_zeroed, 1)
            for s, W in enumerate((W_u, W_i)):
                for half in range(2):
                    act.dma_start(w_blk[half * D:(half + 1) * D, s, half * D:(half + 1) * D], W[:, :]).then_inc(w_in, 16)

            act.wait_ge(eps_ready, 1)
            nc.scalar.activation(root_warm[:, :], eps_sb[:, :], ACT.Sqrt).then_inc(root_warmed, 1)

            def squares(n):
                act.wait_ge(centred, n + 1)
                slot = EGO_SLOT if n < PAIRS else OUT_SLOT
                nc.scalar.activation(work(slot, 2 + n % 2), work(slot, n % 2), ACT.Square).then_inc(squared, 1)

            def root(n):
                act.wait_ge(summed, n + 1)
                nc.scalar.activation(stats[:, n, 3, :], stats[:, n, 2, :], ACT.Sqrt,
                                     bias=eps_sb[:, 0:1], scale=1.0 / D).then_inc(rooted, 1)

            for s in range(PAIRS + 1):
                if s < PAIRS:
                    squares(s)
                    root(s)
                    act.wait_ge(normed, s + 1)
                    nc.scalar.activation(unit(e_sb, s), rows64(work(EGO_SLOT, s % 2)), ACT.Relu).then_inc(ego_ready, 1)
                if s >= 1:
                    act.wait_ge(ego_turned, s)
                    if s >= 3:
                        act.wait_ge(y_ready, s - 2)
                    nc.scalar.activation(work(EGO_SLOT, 4 + (s - 1) % 2), h_ps[s - 1][:, :],
                                         ACT.Copy).then_inc(egoT_ready, 1)

            def slot_back(p, g):
                for b in range(BLOCKS):
                    n = g * BLOCKS + b
                    act.wait_ge(tr_filled, p * (RETAINED * BLOCKS) + (n + 1))
                    src = tr_ps[n % 2][:, :].rearrange("p (r c) -> p r c", r=RB)
                    nc.scalar.activation(slot_columns(g, b), src, ACT.Copy).then_inc(tr_emptied, 1)

            def load_second_half(p, g):
                act.wait_ge(t_summed, p * GROUPS + (g + 1))
                load_second(act, g, p, range(NQ // 2, NQ))

            with act.Fori(0, PANELS) as p:
                for g in range(HELD_BACK):
                    slot_back(p, g)
                for g in range(RETAINED, GROUPS - 1):
                    load_second_half(p, g)
                act.wait_ge(t_summed, p * GROUPS + GROUPS)
                nc.scalar.activation(tT_sb[:, BANK:WIDTH], tT_ps[D:P, :], ACT.Copy).then_inc(tT_ready, 1)
                slot_back(p, HELD_BACK)
                load_second_half(p, GROUPS - 1)

            def hT_copy(k):
                if k < RPAIRS:
                    act.wait_ge(h_summed, (PANELS - 1) * RPAIRS + k + 1)
                else:
                    act.wait_ge(at_used, (PANELS - 1) * (SPAIRS * BLOCKS) + (k - RPAIRS + 1) * BLOCKS)
                if k >= 2:
                    act.wait_ge(h_turned, k - 1)
                nc.scalar.activation(work(OUT_SLOT, 4 + k % 2), h_ps[k][:, :], ACT.Copy).then_inc(hT_ready, 1)

            for k in range(PAIRS + 1):
                if k < PAIRS:
                    hT_copy(k)
                if k >= 1:
                    squares(PAIRS + k - 1)
                    root(PAIRS + k - 1)

        @block.vector
        def _(dve):
            chain = [0]

            def link(ins):
                chain[0] += 1
                ins.then_inc(vstep, 1)
                dve.wait_ge(vstep, chain[0])

            nc.vector.memset(eps_sb[:, :], EPS).then_inc(eps_ready, 1)

            def centre(n, src, dst):
                link(nc.vector.reduce_sum(stats[:, n, 0, :], src, axis=AX.X))
                link(nc.vector.tensor_scalar(stats[:, n, 1, :], stats[:, n, 0, :], -1.0 / D, None, ALU.mult))
                nc.vector.tensor_tensor(dst, src, per_row(stats[:, n, 1, :]), ALU.add).then_inc(centred, 1)

            def square_sum(n, slot):
                dve.wait_ge(squared, n + 1)
                nc.vector.reduce_sum(stats[:, n, 2, :], rows64(work(slot, 2 + n % 2)), axis=AX.X).then_inc(summed, 1)

            def norm(n, slot):
                dve.wait_ge(rooted, n + 1)
                link(nc.vector.reciprocal(stats[:, n, 4, :], stats[:, n, 3, :]))
                c = rows64(work(slot, n % 2))
                return nc.vector.tensor_tensor(c, c, per_row(stats[:, n, 4, :]), ALU.mult)

            def e_rows(u):
                dve.wait_ge(y_ready, u + 1)
                y = rows64(h_ps[u][:, :])
                scaled = rows64(work(EGO_SLOT, 6))
                if u:
                    dve.wait_ge(e_ready, u)
                link(nc.vector.tensor_tensor(scaled, y, per_row(diag_sb[:, u * UB:(u + 1) * UB]), ALU.mult))
                dve.wait_ge(res_summed, u + 1)
                nc.vector.tensor_tensor(unit(e_sb, u), unit(e_sb, u), scaled, ALU.add).then_inc(e_ready, 1)
                nc.vector.memset(h_ps[u][:, :], 0.0).then_inc(h_zeroed, 1)

            for u in range(PAIRS + 1):
                if u < PAIRS:
                    dve.wait_ge(x_in[u], 16)
                    if u >= 2:
                        dve.wait_ge(ego_ready, u - 1)
                    centre(u, unit(x_sb, u), rows64(work(EGO_SLOT, u % 2)))
                if u == 0:
                    dve.wait_ge(small_in, 16 * 6)
                    link(nc.vector.tensor_tensor(scale_rows[:, :], par_rows[:, 0:1], par_rows[:, 1:2], ALU.mult))
                    nc.vector.tensor_scalar(diag_rows[:, :], diag_rows[:, :], scale_rows[:, 0:1], None,
                                            ALU.mult).then_inc(scale_ready, 1)
                if u < PAIRS:
                    square_sum(u, EGO_SLOT)
                    norm(u, EGO_SLOT).then_inc(normed, 1)
                if u == 1:
                    dve.wait_ge(diag_turned, 1)
                    link(nc.vector.tensor_copy(diag_sb[:, :], tT_ps[:, 0:ALL_BLOCKS]))
                if u >= 1:
                    e_rows(u - 1)

            def take_t(p):
                dve.wait_ge(t_summed, p * GROUPS + GROUPS)
                nc.vector.tensor_copy(tT_sb[:, 0:BANK], tT_ps[0:D, :]).then_inc(tT_ready, 1)
                for n, t in enumerate((t_blocks, t_strided)):
                    dve.wait_ge(t_turned, 2 * p + (n + 1))
                    nc.vector.tensor_copy(t[:, :, :], rows64(tT_ps[:, :])).then_inc(t_ready, 1)

            def turn_second(p, k, b):
                n = (k - RPAIRS) * BLOCKS + b
                if b == 0:
                    for g in (2 * k, 2 * k + 1):
                        dve.wait_ge(second_in[g], p * (16 * NQ) + 16 * NQ)
                if n >= RING:
                    dve.wait_ge(at_used, p * (SPAIRS * BLOCKS) + (n + 1 - RING))
                nc.vector.transpose(at_ring[:, n % RING, :, :].rearrange("p g (m c) -> p (g m) c", c=Q),
                                    slots_second(k, b)).then_inc(at_filled, 1)

            with dve.Fori(0, PANELS - 1) as p:
                take_t(p)
                for k in range(RPAIRS, PAIRS):
                    for b in range(BLOCKS):
                        turn_second(p, k, b)

            def centre_h(k):
                n = PAIRS + k
                dve.wait_ge(h_turned, k + 1)
                if k == 0:
                    dve.wait_ge(res_ready, PAIRS)
                if k >= 2:
                    dve.wait_ge(out_ready, k - 1)
                h = tr_ps[k % 2][:, :].rearrange("p (r h d) -> p h r d", h=2, d=D)
                link(nc.vector.reduce_sum(stats[:, n, 0, :].rearrange("p (h r) -> p h r", h=2), h, axis=AX.X))
                link(nc.vector.tensor_scalar(stats[:, n, 1, :], stats[:, n, 0, :], -1.0 / D, None, ALU.mult))
                nc.vector.tensor_tensor(
                    work(OUT_SLOT, n % 2).rearrange("p (h r d) -> p h r d", h=2, d=D), h,
                    stats[:, n, 1, :].rearrange("p (h r o) -> p h r o", h=2, o=1).to_broadcast([P, 2, RB, D]),
                    ALU.add).then_inc(centred, 1)

            last = PANELS - 1
            take_t(last)
            for k in range(RPAIRS, PAIRS):
                for b in range(BLOCKS):
                    turn_second(last, k, b)
                    if (k, b) == (RPAIRS, BLOCKS - 1):
                        centre_h(0)
                    if (k, b) == (RPAIRS + 1, 1):
                        square_sum(PAIRS + 0, OUT_SLOT)
                    if (k, b) == (RPAIRS + 1, 3):
                        norm(PAIRS + 0, OUT_SLOT).then_inc(out_normed, 1)
                    if (k, b) == (RPAIRS + 2, 0):
                        centre_h(1)
                    if (k, b) == (RPAIRS + 2, 2):
                        square_sum(PAIRS + 1, OUT_SLOT)
                    if (k, b) == (RPAIRS + 2, 4):
                        norm(PAIRS + 1, OUT_SLOT).then_inc(out_normed, 1)
            for k in range(2, PAIRS):
                centre_h(k)
                square_sum(PAIRS + k, OUT_SLOT)
                if k < PAIRS - 1:
                    norm(PAIRS + k, OUT_SLOT).then_inc(out_normed, 1)
                else:
                    link(norm(PAIRS + k, OUT_SLOT))
                    c = rows64(work(OUT_SLOT, (PAIRS + k) % 2))
                    link(nc.vector.tensor_tensor(c, c, per_column(gamma_sb[:, :]), ALU.mult))
                    nc.vector.tensor_tensor(unit(x_sb, k), unit(x_sb, k), c, ALU.add).then_inc(last_out_ready, 1)

        @block.tensor
        def _(pe):
            def turn_ego(u):
                pe.wait_ge(ego_ready, u + 1)
                for j in range(RB):
                    last = nc.tensor.transpose(h_ps[u][:, j * P:(j + 1) * P],
                                               e_sb[:, u * UB + 2 * j:u * UB + 2 * j + 2, :], ident[:, :])
                last.then_inc(ego_turned, 1)

            def times_W(u):
                pe.wait_ge(egoT_ready, u + 1)
                for j in range(RB):
                    last = nc.tensor.matmul(h_ps[u][:, j * P:(j + 1) * P],
                                            work(EGO_SLOT, 4 + u % 2)[:, j * P:(j + 1) * P],
                                            w_blk[:, 0 if u < USER_PAIRS else 1, :], start=True, stop=True)
                last.then_inc(y_ready, 1)

            def turn_tiles(p, g, blocks):
                for b in blocks:
                    n = g * BLOCKS + b
                    if n >= 2:
                        pe.wait_ge(tr_emptied, p * (RETAINED * BLOCKS) + (n - 1))
                    for rb in range(RB):
                        last = nc.tensor.transpose(tr_ps[n % 2][:, rb * P:(rb + 1) * P],
                                                   slot_columns(g, b)[:, rb, :], ident[:, :])
                    last.then_inc(tr_filled, 1)

            def sum_t(p, g, turned=None):
                pe.wait_ge(natural_in[g], p * 16 + 16)
                for rb in range(RB):
                    for half in range(2):
                        last = nc.tensor.matmul(tT_ps[half * D:(half + 1) * D, :], e_sb[:, g * RB + rb, :],
                                                slot_natural(g)[:, rb, half * BANK:(half + 1) * BANK],
                                                start=(g == 0 and rb == 0),
                                                stop=(g == GROUPS - 1 and rb == RB - 1))
                    if rb == RB - 1:
                        last.then_inc(t_summed, 1)
                    if turned is not None:
                        turn_tiles(p, turned, (2 * rb, 2 * rb + 1))

            def turn_t(columns):
                for b in range(BLOCKS):
                    last = nc.tensor.transpose(tT_ps[:, b * D:(b + 1) * D], columns(b), ident[0:D, 0:D])
                last.then_inc(t_turned, 1)

            def finish_t(p):
                turn_tiles(p, HELD_BACK, range(0, BLOCKS // 2 - 1))
                pe.wait_ge(tT_ready, 2 * p + 2)
                turn_tiles(p, HELD_BACK, range(BLOCKS // 2 - 1, BLOCKS // 2))
                turn_t(lambda b: tT_sb[:, b * P:(b + 1) * P])
                turn_tiles(p, HELD_BACK, range(BLOCKS // 2, BLOCKS))

            def sum_h(p, k):
                if k == 0:
                    pe.wait_ge(t_ready, 2 * p + 1)
                if k == RPAIRS:
                    pe.wait_ge(t_ready, 2 * p + 2)
                if k < RPAIRS:
                    pe.wait_ge(tr_emptied, p * (RETAINED * BLOCKS) + (2 * k + 2) * BLOCKS)
                for b in range(BLOCKS):
                    n = (k - RPAIRS) * BLOCKS + b
                    if k >= RPAIRS:
                        pe.wait_ge(at_filled, p * (SPAIRS * BLOCKS) + (n + 1))
                    for half in range(2):
                        if k < RPAIRS:
                            t, tile = t_blocks, slot_columns(2 * k + half, b)
                        else:
                            t, tile = t_strided, at_ring[:, n % RING, half, :]
                        last = nc.tensor.matmul(h_ps[k][half * D:(half + 1) * D, :], t[:, b, :], tile,
                                                start=False, stop=True, skip_group_check=True)
                    if k >= RPAIRS:
                        last.then_inc(at_used, 1)
                if k < RPAIRS:
                    last.then_inc(h_summed, 1)
                if k == 0:
                    turn_t(lambda b: tT_sb[:, :].rearrange("d (c b) -> d c b", b=BLOCKS)[:, :, b])

            pe.wait_ge(ident_ready, 1)
            turn_ego(0)
            pe.wait_ge(scale_ready, 1)
            nc.tensor.transpose(tT_ps[:, 0:ALL_BLOCKS], diag_rows[:, :],
                                ident[0:ALL_BLOCKS, 0:ALL_BLOCKS]).then_inc(diag_turned, 1)
            pe.wait_ge(w_in, 16 * 4)
            for g in range(GROUPS):
                if g < PAIRS:
                    times_W(g)
                    if g + 1 < PAIRS:
                        turn_ego(g + 1)
                if g % 2 == 0:
                    pe.wait_ge(e_ready, g // 2 + 1)
                sum_t(0, g, g - PAIRS + 1 if PAIRS - 1 <= g < PAIRS - 1 + HELD_BACK else None)
            finish_t(0)
            pe.wait_ge(h_zeroed, PAIRS)

            with pe.Fori(0, PANELS - 1) as p:
                for k in range(PAIRS):
                    sum_h(p, k)
                for g in range(GROUPS):
                    sum_t(p + 1, g, g - 1 if 1 <= g <= HELD_BACK else None)
                finish_t(p + 1)

            for k in range(PAIRS + 1):
                if k < PAIRS:
                    sum_h(PANELS - 1, k)
                if k >= 1:
                    pe.wait_ge(hT_ready, k)
                    if k >= 3:
                        pe.wait_ge(centred, PAIRS + k - 2)
                    for rb in range(RB):
                        last = nc.tensor.transpose(tr_ps[(k - 1) % 2][:, rb * P:(rb + 1) * P],
                                                   work(OUT_SLOT, 4 + (k - 1) % 2)[:, rb * P:(rb + 1) * P],
                                                   ident[:, :])
                    last.then_inc(h_turned, 1)


_INS = ['x', 'adj', 'L0_gnn_W_u', 'L0_gnn_diag_u', 'L0_gnn_par_u', 'L0_gnn_W_i', 'L0_gnn_diag_i',
        'L0_gnn_par_i', 'L0_gnn_ln_gamma', 'L0_gnn_ln_beta']
_OUTS = [((5120, 64), 'float32')]


def kernel(**inputs):
    import numpy as _np
    import concourse.bacc as _bacc
    from concourse import mybir as _mybir
    from concourse.bass_utils import run_bass_kernel_spmd as _run

    nc = _bacc.Bacc("TRN2", target_bir_lowering=False, num_devices=1,
                    dynamic_dma_scratch_size=1024)
    arrays, args = {}, []
    for name in _INS:
        a = _np.ascontiguousarray(inputs[name])
        arrays[f"in_{name}_dram"] = a
        args.append(nc.dram_tensor(f"in_{name}_dram", a.shape, _mybir.dt.from_np(a.dtype), kind="ExternalInput").ap())
    for i, (shape, dtype) in enumerate(_OUTS):
        dt = _mybir.dt.from_np(_np.dtype(dtype))
        args.append(nc.dram_tensor(f"out_{i}_dram", shape, dt, kind="ExternalOutput").ap())
    gnn_layer_kernel(nc, *args)
    r = _run(nc, [arrays], core_ids=[0])
    return r.results[0]["out_0_dram"]
```

```python
import concourse.bass as bass
from concourse import mybir
from contextlib import ExitStack


def gnn_layer_kernel(nc, x, adj, W_u, diag_u, par_u, W_i, diag_i, par_i, gamma, beta, out):
    fp32 = mybir.dt.float32
    ALU = mybir.AluOpType
    ACT = mybir.ActivationFunctionType
    AX = mybir.AxisListType

    P = 128
    Q = 32
    NQ = P // Q
    N, D = x.shape
    BANK = 512
    ROWS = BANK
    GROUPS = N // ROWS
    PAIRS = GROUPS // 2
    RB = ROWS // P
    WIDTH = 2 * BANK
    PANELS = N // WIDTH
    BLOCKS = WIDTH // P
    SEG = WIDTH // NQ
    BY_PE = (4, 3, 3)
    BY_DVE = (2, 2, 2)
    EARLY_UNITS = (3, 4, 4)
    UNIT = BLOCKS // 2
    UNITS = tuple(groups * BLOCKS // UNIT for groups in BY_DVE)
    RETAINED = tuple(pe + dve for pe, dve in zip(BY_PE, BY_DVE))
    HELD_TILES = BLOCKS // 2
    RING = 6
    PLACES = 2 * RING // UNIT
    EARLY = 4
    FIRST_LAG = 3
    USER_GROUPS = diag_u.shape[0] // ROWS
    USER_PAIRS = USER_GROUPS // 2
    USER_BLOCKS = USER_GROUPS * RB
    ALL_BLOCKS = GROUPS * RB
    UB = 2 * RB
    EPS = 1e-5

    ctx = ExitStack()
    with ctx:
        def sb(name, shape, dt=fp32):
            return ctx.enter_context(nc.sbuf_tensor(name, shape, dt))

        def pb(name, shape, dt=fp32):
            return ctx.enter_context(nc.psum_tensor(name, shape, dt))

        def sem(name):
            return ctx.enter_context(nc.semaphore(name))

        panel = sb("panel", [P, GROUPS, RB * WIDTH])
        x_sb = sb("x_sb", [P, ALL_BLOCKS, D])
        e_sb = sb("e_sb", [P, ALL_BLOCKS, D])
        at_ring = sb("at_ring", [P, RING, 2, ROWS])
        tT_sb = sb("tT_sb", [D, WIDTH])
        t_blocks = sb("t_blocks", [P, BLOCKS, D])
        t_strided = sb("t_strided", [P, BLOCKS, D])
        ident = sb("ident", [P, P])
        w_blk = sb("w_blk", [P, 2, P])
        c_blk = sb("c_blk", [P, P])
        cg_blk = sb("cg_blk", [P, P])
        diag_sb = sb("diag_sb", [P, ALL_BLOCKS])
        par_sb = sb("par_sb", [P, 2, 2])
        par_product = sb("par_product", [P, 2, 1])
        gamma_sb = sb("gamma_sb", [P, D])
        beta_sb = sb("beta_sb", [P, D])
        eps_sb = sb("eps_sb", [P, 1])
        ones_sb = sb("ones_sb", [P, 1])
        root_warm = sb("root_warm", [P, 1])
        stats = sb("stats", [P, 2 * PAIRS, 5, UB])

        h_ps = [pb(f"h_ps{k}", [P, BANK]) for k in range(PAIRS)]
        tT_ps = pb("tT_ps", [P, BANK])
        tr_ps = [pb(f"tr_ps{k}", [P, BANK]) for k in range(2)]

        x_in = [sem(f"x_in{u}") for u in range(PAIRS)]
        diag_in = sem("diag_in")
        affine_in = sem("affine_in")
        w_in = sem("w_in")
        w_zeroed = sem("w_zeroed")
        eps_ready = sem("eps_ready")
        ones_ready = sem("ones_ready")
        ident_ready = sem("ident_ready")
        c_ready = sem("c_ready")
        centred = sem("centred")
        squared = sem("squared")
        summed = sem("summed")
        rooted = sem("rooted")
        normed = sem("normed")
        root_warmed = sem("root_warmed")
        ego_ready = sem("ego_ready")
        ego_turned = sem("ego_turned")
        egoT_ready = sem("egoT_ready")
        y_ready = sem("y_ready")
        res_summed = sem("res_summed")
        res_ready = sem("res_ready")
        e_ready = sem("e_ready")
        h_zeroed = sem("h_zeroed")
        natural_in = [sem(f"natural_in{g}") for g in range(GROUPS)]
        second_in = [sem(f"second_in{g}") for g in range(GROUPS)]
        t_summed = sem("t_summed")
        tr_filled = sem("tr_filled")
        tr_emptied = sem("tr_emptied")
        tT_ready = sem("tT_ready")
        t_turned = sem("t_turned")
        t_ready = sem("t_ready")
        at_filled = sem("at_filled")
        at_used = sem("at_used")
        unit_turned = sem("unit_turned")
        unit_back = sem("unit_back")
        h_summed = sem("h_summed")
        hT_ready = sem("hT_ready")
        h_turned = sem("h_turned")
        out_ready = sem("out_ready")
        last_out_ready = sem("last_out_ready")
        out_normed = sem("out_normed")
        out_scaled = sem("out_scaled")
        stored = sem("stored")
        vstep = sem("vstep")
        pstep = sem("pstep")

        LAST = PANELS - 1

        def of_panel(values, p):
            return (values[0] if p == 0 else values[2]) if isinstance(p, int) else values[1]

        def by_pe(p):
            return of_panel(BY_PE, p)

        def units(p):
            return of_panel(UNITS, p)

        def retained(p):
            return by_pe(p) + of_panel(BY_DVE, p)

        def full_pairs(p):
            return retained(p) // 2

        def before(p, values):
            return 0 if isinstance(p, int) and p == 0 else p * values[1] + (values[0] - values[1])

        def tiles_before(p):
            return before(p, [groups * BLOCKS for groups in BY_PE])

        def units_before(p):
            return before(p, UNITS)

        def pairs_before(p):
            return before(p, [groups // 2 for groups in RETAINED])

        def entries_before(p):
            return before(p, [(PAIRS - groups // 2) * BLOCKS for groups in RETAINED])

        def seconds_before(p, g):
            return before(p, [16 * NQ * int(g >= groups) for groups in RETAINED])

        def slot_natural(g):
            return panel[:, g, :].rearrange("p (r c) -> p r c", r=RB)

        def slot_columns(g, b):
            return slot_natural(g)[:, :, b * P:(b + 1) * P]

        def slots_second(k, b, halves):
            pair = panel[:, 2 * k + halves.start:2 * k + halves.stop, :].rearrange("p g (m c b) -> p (g m) c b", c=Q, b=BLOCKS)
            return pair[:, :, :, b]

        def unit_of(p, j):
            return by_pe(p) + j * UNIT // BLOCKS, j * UNIT % BLOCKS

        def unit_tiles(j):
            j = j % PLACES
            return at_ring[:, :, :, :].rearrange("p e h i -> p (e h) i")[:, j * UNIT:(j + 1) * UNIT, :]

        def work(g, k):
            return panel[:, g, k * BANK:(k + 1) * BANK]

        def rows64(ap):
            return ap.rearrange("p (n d) -> p n d", d=D)

        def by_group(bank):
            return bank[:, :].rearrange("p (r h d) -> p h r d", h=2, d=D)

        def per_row(ap):
            return ap.rearrange("p (n o) -> p n o", o=1).to_broadcast([P, UB, D])

        def per_column(ap):
            return ap.rearrange("p (o d) -> p o d", o=1).to_broadcast([P, UB, D])

        def unit(t, u):
            return t[:, u * UB:(u + 1) * UB, :]

        def load_natural(eng, g, p):
            src = adj[g * ROWS:(g + 1) * ROWS, bass.ds(p * WIDTH, WIDTH)]
            eng.dma_start(slot_natural(g), src.rearrange("(p r) c -> p r c", p=P)).then_inc(natural_in[g], 16)

        def load_second(eng, g, p, quadrants):
            for q in quadrants:
                src = adj[g * ROWS:(g + 1) * ROWS, bass.ds(p * WIDTH + q * SEG, SEG)]
                dst = panel[q * Q:(q + 1) * Q, g, :].rearrange("p (m c) -> p m c", c=SEG)
                eng.dma_start(dst, src.rearrange("(m p) c -> p m c", p=Q)).then_inc(second_in[g], 16)

        EGO_SLOT = GROUPS - 1
        OUT_SLOT = 0

        last_squares = work(OUT_SLOT, 3).rearrange("p (h r d) -> p h r d", h=2, d=D)

        last_bank = (tr_ps[(PAIRS - 1) % 2], h_ps[0])

        def last_part(ap, part):
            return ap[:, :, part * (RB // 2):(part + 1) * (RB // 2)]

        block = ctx.enter_context(nc.Block())

        @block.sync
        def _(sp):
            def load_x(u):
                src = x[u * 2 * ROWS:(u + 1) * 2 * ROWS, :].rearrange("(g p r) d -> p g (r d)", p=P, r=RB)
                dst = unit(x_sb, u).rearrange("p (g r) d -> p g (r d)", r=RB)
                sp.dma_start(dst, src).then_inc(x_in[u], 16)

            load_x(0)
            load_natural(sp, 0, 0)
            sp.wait_ge(w_zeroed, 1)
            for s, W in enumerate((W_u, W_i)):
                for half in range(2):
                    sp.dma_start(w_blk[half * D:(half + 1) * D, s, half * D:(half + 1) * D], W[:, :]).then_inc(w_in, 16)
            for u in range(1, PAIRS):
                load_x(u)
            for g in range(1, GROUPS):
                if g == EGO_SLOT:
                    sp.wait_ge(e_ready, PAIRS)
                load_natural(sp, g, 0)

            def second_loads(p):
                for g in range(retained(p), GROUPS):
                    sp.wait_ge(t_summed, p * GROUPS + (g + 1))
                    load_second(sp, g, p, range(0, NQ // 2))

            def next_natural_loads(p):
                for g in range(GROUPS):
                    if g < 2 * full_pairs(p):
                        sp.wait_ge(h_summed, pairs_before(p) + (g // 2 + 1))
                    elif g < retained(p):
                        sp.wait_ge(at_used, entries_before(p) + BLOCKS)
                    else:
                        sp.wait_ge(at_filled, entries_before(p) + (g // 2 - full_pairs(p) + 1) * BLOCKS)
                    load_natural(sp, g, p + 1)

            second_loads(0)
            next_natural_loads(0)
            with sp.Fori(1, LAST) as p:
                second_loads(p)
                next_natural_loads(p)
            second_loads(LAST)
            for k in range(PAIRS):
                if k < PAIRS - 1:
                    sp.wait_ge(out_ready, k + 1)
                for half in range(2):
                    if k == PAIRS - 1:
                        sp.wait_ge(last_out_ready, half + 1)
                    g = 2 * k + half
                    dst = out[g * ROWS:(g + 1) * ROWS, :].rearrange("(p r) d -> p (r d)", p=P)
                    src = x_sb[:, g * RB:(g + 1) * RB, :].rearrange("p r d -> p (r d)")
                    sp.dma_start(dst, src).then_inc(stored, 16)
            sp.wait_ge(stored, 16 * 2 * PAIRS)

        @block.gpsimd
        def _(pool):
            pool.memset(w_blk[:, :, :], 0.0).then_inc(w_zeroed, 1)
            pool.memset(ident[:, :], 0.0).then_inc(pstep, 1)
            pool.memset(ones_sb[:, :], 1.0).then_inc(ones_ready, 1)
            pool.wait_ge(pstep, 1)
            pool.affine_select(out=ident[:, :], in_=ident[:, :], compare_op=ALU.not_equal, fill=1.0,
                               base=0, pattern=[[-1, P]], channel_multiplier=1).then_inc(ident_ready, 1)
            for u in range(PAIRS):
                pool.wait_ge(ego_ready, u + 1)
                pool.tensor_tensor(unit(x_sb, u), unit(x_sb, u), unit(e_sb, u), ALU.add).then_inc(res_summed, 1)

            def units_back(p):
                for j in range(units(p)):
                    g, b = unit_of(p, j)
                    if b == 0:
                        pool.wait_ge(t_summed, p * GROUPS + (g + 1))
                    pool.wait_ge(unit_turned, units_before(p) + (j + 1))
                    dst = slot_natural(g)[:, :, b * P:(b + UNIT) * P].rearrange("c s (b i) -> c b s i", i=P)
                    src = unit_tiles(j).rearrange("c b (s i) -> c b s i", i=P)
                    one = ones_sb[:, :].rearrange("p (b s i) -> p b s i", b=1, s=1).to_broadcast([P, UNIT, RB, P])
                    pool.tensor_tensor(dst, src, one, ALU.mult).then_inc(unit_back, 1)

            pool.wait_ge(ones_ready, 1)
            units_back(0)
            pool.wait_ge(affine_in, 16 * 2)
            for u in range(PAIRS):
                pool.wait_ge(res_summed, u + 1)
                pool.tensor_tensor(unit(x_sb, u), unit(x_sb, u), per_column(beta_sb[:, :]),
                                   ALU.add).then_inc(res_ready, 1)
            pool.memset(c_blk[:, :], 0.0).then_inc(pstep, 1)
            pool.wait_ge(pstep, 2)
            for half in range(2):
                pool.memset(c_blk[half * D:(half + 1) * D, half * D:(half + 1) * D], -1.0 / D).then_inc(pstep, 1)
            pool.wait_ge(pstep, 4)
            pool.wait_ge(ident_ready, 1)
            pool.tensor_tensor(c_blk[:, :], c_blk[:, :], ident[:, :], ALU.add).then_inc(pstep, 1)
            pool.wait_ge(pstep, 5)
            pool.tensor_tensor(cg_blk[:, :].rearrange("p (h d) -> p h d", h=2),
                               c_blk[:, :].rearrange("p (h d) -> p h d", h=2),
                               gamma_sb[:, :].rearrange("p (o d) -> p o d", o=1).to_broadcast([P, 2, D]),
                               ALU.mult).then_inc(c_ready, 1)

            with pool.Fori(1, LAST) as p:
                units_back(p)
            units_back(LAST)

            for k in range(PAIRS - 1):
                c = rows64(work(OUT_SLOT, k % 2))
                pool.wait_ge(out_normed, 2 * k + 2)
                pool.tensor_tensor(c, c, per_column(gamma_sb[:, :]), ALU.mult).then_inc(out_scaled, 1)
                pool.wait_ge(out_scaled, k + 1)
                pool.tensor_tensor(unit(x_sb, k), unit(x_sb, k), c, ALU.add).then_inc(out_ready, 1)

        @block.scalar
        def _(act):
            for n, par in enumerate((par_u, par_i)):
                act.dma_start(par_sb[:, n, :], par.rearrange("(o n) -> o n", o=1).to_broadcast([P, 2])).then_inc(diag_in, 16)
            for blocks, diag in ((slice(0, USER_BLOCKS), diag_u), (slice(USER_BLOCKS, ALL_BLOCKS), diag_i)):
                act.dma_start(diag_sb[:, blocks].rearrange("p (g r) -> p g r", r=RB),
                              diag.rearrange("(g p r) -> p g r", p=P, r=RB)).then_inc(diag_in, 16)
            act.wait_ge(eps_ready, 1)
            nc.scalar.activation(root_warm[:, :], eps_sb[:, :], ACT.Sqrt).then_inc(root_warmed, 1)

            def squares(n):
                act.wait_ge(centred, n + 1)
                slot = EGO_SLOT if n < PAIRS else OUT_SLOT
                nc.scalar.activation(work(slot, 2 + n % 2), work(slot, n % 2), ACT.Square).then_inc(squared, 1)

            def root(n):
                act.wait_ge(summed, n + 1)
                nc.scalar.activation(stats[:, n, 3, :], stats[:, n, 2, :], ACT.Sqrt,
                                     bias=eps_sb[:, 0:1], scale=1.0 / D).then_inc(rooted, 1)

            def egoT_copy(u):
                act.wait_ge(ego_turned, u + 1)
                if u >= 2:
                    act.wait_ge(y_ready, u - 1)
                nc.scalar.activation(work(EGO_SLOT, 4 + u % 2), h_ps[u][:, :], ACT.Copy).then_inc(egoT_ready, 1)

            squares(0)
            for u in range(PAIRS):
                if 1 <= u < PAIRS - 1:
                    squares(u + 1)
                root(u)
                act.wait_ge(normed, u + 1)
                nc.scalar.activation(unit(e_sb, u), rows64(work(EGO_SLOT, u % 2)), ACT.Relu).then_inc(ego_ready, 1)
                egoT_copy(u)
                if u == 0:
                    squares(1)
            for t, v in ((gamma_sb, gamma), (beta_sb, beta)):
                act.dma_start(t[:, :], v.rearrange("(o n) -> o n", o=1).to_broadcast([P, D])).then_inc(affine_in, 16)

            def slot_back(p, g, blocks=range(BLOCKS)):
                for b in blocks:
                    n = g * BLOCKS + b
                    act.wait_ge(tr_filled, tiles_before(p) + (n + 1))
                    src = tr_ps[n % 2][:, :].rearrange("c (r s p) -> c s p r", r=RB, s=RB)
                    dst = slot_columns(g, b).rearrange("c s (p r) -> c s p r", r=RB)
                    nc.scalar.activation(dst, src, ACT.Copy).then_inc(tr_emptied, 1)

            def load_second_half(p, g):
                act.wait_ge(t_summed, p * GROUPS + (g + 1))
                load_second(act, g, p, range(NQ // 2, NQ))

            def panel_of_act(p):
                held_back = by_pe(p) - 1
                for g in range(held_back):
                    slot_back(p, g)
                slot_back(p, held_back, range(HELD_TILES))
                for g in range(retained(p), GROUPS - 1):
                    load_second_half(p, g)
                act.wait_ge(t_summed, p * GROUPS + GROUPS)
                nc.scalar.activation(tT_sb[:, BANK:WIDTH], tT_ps[D:P, :], ACT.Copy).then_inc(tT_ready, 1)
                slot_back(p, held_back, range(HELD_TILES, BLOCKS))
                load_second_half(p, GROUPS - 1)

            panel_of_act(0)
            with act.Fori(1, LAST) as p:
                panel_of_act(p)
            panel_of_act(LAST)

            def squares_h(k):
                n = PAIRS + k
                act.wait_ge(h_turned, k + 1)
                for half in range(2):
                    for r in range(RB):
                        j = half * RB + r
                        last = nc.scalar.activation(work(OUT_SLOT, 2)[:, j * D:(j + 1) * D],
                                                    by_group(tr_ps[k % 2])[:, half, r, :], ACT.Square,
                                                    accum_out=stats[:, n, 2, j:j + 1])
                last.then_inc(squared, 1)
                act.wait_ge(squared, n + 1)
                nc.scalar.activation(stats[:, n, 3, :], stats[:, n, 2, :], ACT.Sqrt,
                                     bias=eps_sb[:, 0:1], scale=1.0 / D).then_inc(rooted, 1)

            def hT_copy(k):
                if k < full_pairs(LAST):
                    act.wait_ge(h_summed, pairs_before(LAST) + (k + 1))
                else:
                    act.wait_ge(at_used, entries_before(LAST) + (k - full_pairs(LAST) + 1) * BLOCKS)
                if k >= 2:
                    act.wait_ge(h_turned, k - 1)
                nc.scalar.activation(work(OUT_SLOT, 4 + k % 2), h_ps[k][:, :], ACT.Copy).then_inc(hT_ready, 1)

            hT_copy(0)
            for k in range(1, PAIRS):
                squares_h(k - 1)
                hT_copy(k)
            n = 2 * PAIRS - 1
            for part in range(2):
                act.wait_ge(h_turned, PAIRS + part)
                nc.scalar.activation(last_part(last_squares, part), last_part(by_group(last_bank[part]), part),
                                     ACT.Square).then_inc(squared, 1)
            act.wait_ge(summed, PAIRS + 2)
            nc.scalar.activation(stats[:, n, 3, :], stats[:, n, 2, :], ACT.Sqrt,
                                 bias=eps_sb[:, 0:1], scale=1.0 / D).then_inc(rooted, 1)

        @block.vector
        def _(dve):
            chain = [0]

            def link(ins):
                chain[0] += 1
                ins.then_inc(vstep, 1)
                dve.wait_ge(vstep, chain[0])

            nc.vector.memset(eps_sb[:, :], EPS).then_inc(eps_ready, 1)

            def centre(n, src, dst):
                link(nc.vector.reduce_sum(stats[:, n, 0, :], src, axis=AX.X))
                link(nc.vector.tensor_scalar(stats[:, n, 1, :], stats[:, n, 0, :], -1.0 / D, None, ALU.mult))
                nc.vector.tensor_tensor(dst, src, per_row(stats[:, n, 1, :]), ALU.add).then_inc(centred, 1)

            def square_sum(n, slot):
                dve.wait_ge(squared, n + 1)
                nc.vector.reduce_sum(stats[:, n, 2, :], rows64(work(slot, 2 + n % 2)), axis=AX.X).then_inc(summed, 1)

            def norm(n, slot):
                dve.wait_ge(rooted, n + 1)
                link(nc.vector.reciprocal(stats[:, n, 4, :], stats[:, n, 3, :]))
                c = rows64(work(slot, n % 2))
                return nc.vector.tensor_tensor(c, c, per_row(stats[:, n, 4, :]), ALU.mult)

            def e_rows(u):
                dve.wait_ge(y_ready, u + 1)
                y = rows64(h_ps[u][:, :])
                scaled = rows64(work(EGO_SLOT, 6))
                if u:
                    dve.wait_ge(e_ready, u)
                link(nc.vector.tensor_tensor(scaled, y, per_row(diag_sb[:, u * UB:(u + 1) * UB]), ALU.mult))
                dve.wait_ge(res_summed, u + 1)
                nc.vector.tensor_tensor(unit(e_sb, u), unit(e_sb, u), scaled, ALU.add).then_inc(e_ready, 1)
                nc.vector.memset(h_ps[u][:, :], 0.0).then_inc(h_zeroed, 1)

            def centre_x(u):
                dve.wait_ge(x_in[u], 16)
                if u >= 2:
                    dve.wait_ge(ego_ready, u - 1)
                centre(u, unit(x_sb, u), rows64(work(EGO_SLOT, u % 2)))

            centre_x(0)
            square_sum(0, EGO_SLOT)
            norm(0, EGO_SLOT).then_inc(normed, 1)
            dve.wait_ge(diag_in, 16 * 4)
            link(nc.vector.tensor_tensor(par_product[:, :, :], par_sb[:, :, 0:1], par_sb[:, :, 1:2], ALU.mult))
            for n, blocks in enumerate((slice(0, USER_BLOCKS), slice(USER_BLOCKS, ALL_BLOCKS))):
                link(nc.vector.tensor_scalar(diag_sb[:, blocks], diag_sb[:, blocks], par_product[:, n, :],
                                             None, ALU.mult))

            def turn_units(p, some):
                for j in some:
                    g, b = unit_of(p, j)
                    if j == 0 and not (isinstance(p, int) and p == 0):
                        dve.wait_ge(at_used, entries_before(p))
                    if j >= PLACES:
                        dve.wait_ge(unit_back, units_before(p) + (j + 1 - PLACES))
                    if b == 0:
                        dve.wait_ge(natural_in[g], p * 16 + 16)
                    for rows in range(NQ):
                        for cols in range(NQ):
                            src = slot_natural(g)[rows * Q:(rows + 1) * Q, :, b * P:(b + UNIT) * P]
                            src = src.rearrange("p r (b q c) -> p b r q c", b=UNIT, q=NQ)[:, :, :, cols, :]
                            dst = unit_tiles(j)[cols * Q:(cols + 1) * Q, :, :]
                            dst = dst.rearrange("c b (q j r) -> c b r q j", q=NQ, r=RB)[:, :, :, rows, :]
                            turned = nc.vector.transpose(dst, src)
                    turned.then_inc(unit_turned, 1)

            centre_x(1)
            e_rows(0)
            for u in range(1, PAIRS):
                if u + 1 < PAIRS:
                    centre_x(u + 1)
                square_sum(u, EGO_SLOT)
                norm(u, EGO_SLOT).then_inc(normed, 1)
                if u >= 2:
                    e_rows(u - 1)


            def take_tT(p):
                dve.wait_ge(t_summed, p * GROUPS + GROUPS)
                nc.vector.tensor_copy(tT_sb[:, 0:BANK], tT_ps[0:D, :]).then_inc(tT_ready, 1)
                take_t(p, 0, t_blocks)

            def take_t(p, n, t):
                dve.wait_ge(t_turned, 2 * p + (n + 1))
                nc.vector.tensor_copy(t[:, :, :], rows64(tT_ps[:, :])).then_inc(t_ready, 1)

            def wait_second(p, g):
                dve.wait_ge(second_in[g], seconds_before(p, g) + 16 * NQ)

            def second_halves(p, k):
                return slice(max(retained(p) - 2 * k, 0), 2)

            def wait_pair(p, k):
                for half in range(second_halves(p, k).start, 2):
                    wait_second(p, 2 * k + half)

            def turn_second(p, k, b, halves):
                n = (k - full_pairs(p)) * BLOCKS + b
                if n >= RING:
                    dve.wait_ge(at_used, entries_before(p) + (n + 1 - RING))
                turned = nc.vector.transpose(at_ring[:, n % RING, halves, :].rearrange("p g (m c) -> p (g m) c", c=Q),
                                             slots_second(k, b, halves))
                if halves.stop == 2:
                    turned.then_inc(at_filled, 1)

            def panel_of_dve(p):
                early = of_panel(EARLY_UNITS, p)
                if isinstance(p, int) and p == 0:
                    turn_units(0, range(1))
                    e_rows(PAIRS - 1)
                    turn_units(0, range(1, early))
                else:
                    turn_units(p, range(early))
                take_tT(p)
                turn_units(p, range(early, units(p)))
                dve.wait_ge(unit_back, units_before(p) + units(p))
                for k in range(full_pairs(p), PAIRS):
                    wait_pair(p, k)
                    for b in range(BLOCKS):
                        if (k, b) == (full_pairs(p), EARLY):
                            take_t(p, 1, t_strided)
                        turn_second(p, k, b, second_halves(p, k))

            panel_of_dve(0)
            with dve.Fori(1, LAST) as p:
                panel_of_dve(p)

            def scaled_rows(n, bank, half, dst):
                rstd = stats[:, n, 4, half * RB:(half + 1) * RB].rearrange("p (r o) -> p r o", o=1)
                return nc.vector.tensor_tensor(dst.rearrange("p (h r) d -> p h r d", h=2)[:, half, :, :],
                                               by_group(bank)[:, half, :, :], rstd.to_broadcast([P, RB, D]), ALU.mult)

            def norm_h(k):
                n = PAIRS + k
                dve.wait_ge(rooted, n + 1)
                link(nc.vector.reciprocal(stats[:, n, 4, :], stats[:, n, 3, :]))
                if k >= 2:
                    dve.wait_ge(out_ready, k - 1)
                for half in range(2):
                    scaled_rows(n, tr_ps[k % 2], half, rows64(work(OUT_SLOT, k % 2))).then_inc(out_normed, 1)

            turn_units(LAST, range(EARLY_UNITS[2]))
            take_tT(LAST)
            turn_units(LAST, range(EARLY_UNITS[2], units(LAST)))
            dve.wait_ge(unit_back, units_before(LAST) + units(LAST))
            for k in range(full_pairs(LAST), PAIRS - 1):
                wait_pair(LAST, k)
                for b in range(BLOCKS):
                    if (k, b) == (PAIRS - 3, BLOCKS - 2):
                        norm_h(0)
                    if (k, b) == (full_pairs(LAST), EARLY):
                        take_t(LAST, 1, t_strided)
                    turn_second(LAST, k, b, second_halves(LAST, k))
            norm_h(1)
            for half in range(2):
                wait_second(LAST, GROUPS - 2 + half)
                for b in range(RING // 2):
                    turn_second(LAST, PAIRS - 1, b, slice(half, half + 1))
            for b in range(RING // 2, BLOCKS):
                if b == BLOCKS - 2:
                    norm_h(2)
                turn_second(LAST, PAIRS - 1, b, slice(0, 2))
            norm_h(3)
            n = 2 * PAIRS - 1
            for part in range(2):
                dve.wait_ge(squared, n + 1 + part)
                nc.vector.reduce_sum(last_part(stats[:, n, 2, :].rearrange("p (h r) -> p h r", h=2), part),
                                     last_part(last_squares, part), axis=AX.X).then_inc(summed, 1)
            dve.wait_ge(rooted, n + 1)
            link(nc.vector.reciprocal(stats[:, n, 4, :], stats[:, n, 3, :]))
            dve.wait_ge(h_turned, PAIRS + 2)
            dve.wait_ge(res_ready, PAIRS)
            for half in range(2):
                last = scaled_rows(n, tT_ps, half, rows64(work(OUT_SLOT, 6)))
            link(last)
            for half in range(2):
                g = GROUPS - 2 + half
                nc.vector.tensor_tensor(x_sb[:, g * RB:(g + 1) * RB, :], x_sb[:, g * RB:(g + 1) * RB, :],
                                        rows64(work(OUT_SLOT, 6))[:, half * RB:(half + 1) * RB, :],
                                        ALU.add).then_inc(last_out_ready, 1)

        @block.tensor
        def _(pe):
            def turn_ego(u):
                pe.wait_ge(ego_ready, u + 1)
                for j in range(RB):
                    last = nc.tensor.transpose(h_ps[u][:, j * P:(j + 1) * P],
                                               e_sb[:, u * UB + 2 * j:u * UB + 2 * j + 2, :], ident[:, :])
                last.then_inc(ego_turned, 1)

            def times_W(u):
                pe.wait_ge(egoT_ready, u + 1)
                for j in range(RB):
                    last = nc.tensor.matmul(h_ps[u][:, j * P:(j + 1) * P],
                                            work(EGO_SLOT, 4 + u % 2)[:, j * P:(j + 1) * P],
                                            w_blk[:, 0 if u < USER_PAIRS else 1, :], start=True, stop=True)
                last.then_inc(y_ready, 1)

            def turn_tiles(p, g, blocks):
                for b in blocks:
                    n = g * BLOCKS + b
                    if n >= 2:
                        pe.wait_ge(tr_emptied, tiles_before(p) + (n - 1))
                    for rb in range(RB):
                        last = nc.tensor.transpose(tr_ps[n % 2][:, rb * P:(rb + 1) * P],
                                                   slot_columns(g, b)[:, rb, :], ident[:, :])
                    last.then_inc(tr_filled, 1)

            def tiles_beside(p, g):
                if 1 <= g < by_pe(p):
                    return g - 1, range(BLOCKS)
                if g == by_pe(p):
                    return g - 1, range(HELD_TILES)
                return None, ()

            def sum_t(p, g, turned, blocks):
                pe.wait_ge(natural_in[g], p * 16 + 16)
                for rb in range(RB):
                    for half in range(2):
                        last = nc.tensor.matmul(tT_ps[half * D:(half + 1) * D, :], e_sb[:, g * RB + rb, :],
                                                slot_natural(g)[:, rb, half * BANK:(half + 1) * BANK],
                                                start=(g == 0 and rb == 0),
                                                stop=(g == GROUPS - 1 and rb == RB - 1))
                    if rb == RB - 1:
                        last.then_inc(t_summed, 1)
                    turn_tiles(p, turned, blocks[len(blocks) * rb // RB:len(blocks) * (rb + 1) // RB])

            def turn_t(columns):
                for b in range(BLOCKS):
                    last = nc.tensor.transpose(tT_ps[:, b * D:(b + 1) * D], columns(b), ident[0:D, 0:D])
                last.then_inc(t_turned, 1)

            def finish_t(p):
                held_back = by_pe(p) - 1
                turn_tiles(p, held_back, range(HELD_TILES, HELD_TILES + 1))
                pe.wait_ge(tT_ready, 2 * p + 2)
                turn_tiles(p, held_back, range(HELD_TILES + 1, HELD_TILES + 2))
                turn_t(lambda b: tT_sb[:, b * P:(b + 1) * P])
                turn_tiles(p, held_back, range(HELD_TILES + 2, BLOCKS))

            def rows_of_h(k):
                pe.wait_ge(hT_ready, k + 1)
                if k >= 2:
                    pe.wait_ge(out_normed, 2 * (k - 1))
                if k == 0:
                    pe.wait_ge(c_ready, 1)
                rows = work(OUT_SLOT, 4 + k % 2).rearrange("d (p r) -> d r p", r=RB)
                for matrix, bank in ((c_blk, tr_ps[k % 2]), (cg_blk, tT_ps))[:1 if k < PAIRS - 1 else 2]:
                    for rb in range(RB):
                        if k == PAIRS - 1 and matrix is c_blk:
                            bank = last_bank[rb * 2 // RB]
                            if rb == RB // 2:
                                last.then_inc(h_turned, 1)
                        last = nc.tensor.matmul(bank[:, rb * P:(rb + 1) * P], rows[:, rb, :], matrix[:, :],
                                                start=True, stop=True)
                    last.then_inc(h_turned, 1)

            def sum_h(p, k, between=None):
                if k == 0:
                    pe.wait_ge(t_ready, 2 * p + 1)
                if k == full_pairs(p):
                    pe.wait_ge(t_ready, 2 * p + 2)
                if 2 * k < by_pe(p):
                    pe.wait_ge(tr_emptied, tiles_before(p) + min(2 * k + 2, by_pe(p)) * BLOCKS)
                if by_pe(p) < 2 * k + 2 and 2 * k < retained(p):
                    groups = min(2 * k + 2, retained(p)) - by_pe(p)
                    pe.wait_ge(unit_back, units_before(p) + groups * BLOCKS // UNIT)
                for b in range(BLOCKS):
                    if b == BLOCKS // 2 and between is not None:
                        rows_of_h(between)
                    n = (k - full_pairs(p)) * BLOCKS + b
                    if k >= full_pairs(p):
                        pe.wait_ge(at_filled, entries_before(p) + (n + 1))
                    for half in range(2):
                        if 2 * k + half < retained(p):
                            t, tile = t_blocks, slot_columns(2 * k + half, b)
                        else:
                            t, tile = t_strided, at_ring[:, n % RING, half, :]
                        last = nc.tensor.matmul(h_ps[k][half * D:(half + 1) * D, :], t[:, b, :], tile,
                                                start=False, stop=True, skip_group_check=True)
                    if k >= full_pairs(p):
                        last.then_inc(at_used, 1)
                if k < full_pairs(p):
                    last.then_inc(h_summed, 1)
                if k == 0:
                    turn_t(lambda b: tT_sb[:, :].rearrange("d (c b) -> d c b", b=BLOCKS)[:, :, b])

            pe.wait_ge(ident_ready, 1)
            turn_ego(0)
            pe.wait_ge(w_in, 16 * 4)
            times_W(0)
            for g in range(GROUPS):
                if 1 <= g < PAIRS:
                    turn_ego(g)
                if g == 1:
                    times_W(1)
                if g % 2 == 0:
                    pe.wait_ge(e_ready, g // 2 + 1)
                sum_t(0, g, *tiles_beside(0, g - FIRST_LAG))
                if 2 <= g < PAIRS:
                    times_W(g)
            finish_t(0)
            pe.wait_ge(h_zeroed, PAIRS)
            for k in range(PAIRS):
                sum_h(0, k)

            def panel_t(p):
                for g in range(GROUPS):
                    sum_t(p, g, *tiles_beside(p, g))
                finish_t(p)

            with pe.Fori(1, LAST) as p:
                panel_t(p)
                for k in range(PAIRS):
                    sum_h(p, k)

            panel_t(LAST)
            for k in range(PAIRS):
                sum_h(LAST, k, k - 1 if k else None)
            rows_of_h(PAIRS - 1)


_INS = ['x', 'adj', 'L0_gnn_W_u', 'L0_gnn_diag_u', 'L0_gnn_par_u', 'L0_gnn_W_i', 'L0_gnn_diag_i',
        'L0_gnn_par_i', 'L0_gnn_ln_gamma', 'L0_gnn_ln_beta']
_OUTS = [((5120, 64), 'float32')]


def kernel(**inputs):
    import numpy as _np
    import concourse.bacc as _bacc
    from concourse import mybir as _mybir
    from concourse.bass_utils import run_bass_kernel_spmd as _run

    nc = _bacc.Bacc("TRN2", target_bir_lowering=False, num_devices=1,
                    dynamic_dma_scratch_size=1024)
    arrays, args = {}, []
    for name in _INS:
        a = _np.ascontiguousarray(inputs[name])
        arrays[f"in_{name}_dram"] = a
        args.append(nc.dram_tensor(f"in_{name}_dram", a.shape, _mybir.dt.from_np(a.dtype), kind="ExternalInput").ap())
    for i, (shape, dtype) in enumerate(_OUTS):
        dt = _mybir.dt.from_np(_np.dtype(dtype))
        args.append(nc.dram_tensor(f"out_{i}_dram", shape, dt, kind="ExternalOutput").ap())
    gnn_layer_kernel(nc, *args)
    r = _run(nc, [arrays], core_ids=[0])
    return r.results[0]["out_0_dram"]
```
